# Optimizing a Trainium2 kernel written in Bass

```python
import numpy as np
import jax
import jax.numpy as jnp

def _softmax(x, axis=-1):
    return jax.nn.softmax(x, axis=axis)

def _gelu(x):
    return jax.nn.gelu(x, approximate=True)

def _silu(x):
    return jax.nn.silu(x)

def _sigmoid(x):
    return jax.nn.sigmoid(x)

def _layernorm(x, axis=-1, eps=1e-05):
    m = jnp.mean(x, axis=axis, keepdims=True)
    v = jnp.var(x, axis=axis, keepdims=True)
    return (x - m) / jnp.sqrt(v + eps)

def _scatter_add(tgt, idx, src, axis=0):
    return tgt.at[idx].add(src)

def _segment_sum(src, seg, n):
    return jax.ops.segment_sum(src, seg, n)
kernel_name = 'mk_cond_resid_d2_seqx_r4_496147'

def setup_inputs(seed: int=0):
    np.random.seed(seed)
    _w = jnp.asarray

    def _rec_inputs():
        import jax
        import jax.numpy as jnp
        _rk = jax.random.key(seed)
        x = 7.22e-05 + 1 * jax.random.normal(jax.random.fold_in(_rk, 1), (16, 256, 512), jnp.float32)
        _lenS = 256 - jax.random.randint(jax.random.fold_in(_rk, 7), (16,), 0, max(1, 256 // 4) + 1, jnp.int32)
        _lenS2 = 256 - jax.random.randint(jax.random.fold_in(_rk, 8), (16,), 0, max(1, 256 // 4) + 1, jnp.int32)
        cond_2048 = jax.random.bernoulli(jax.random.fold_in(_rk, 11), 0.5063, (16, 512)).astype(jnp.float32)
        return (x, cond_2048)
    x, cond_2048 = _rec_inputs()

    def _L0_cond_setup():
        import jax, jax.numpy as jnp
        import numpy as np
        NH = 8
        NEG = -1e+30
        key = jax.random.key(seed)
        k1, k2, k3, k4 = jax.random.split(key, 4)
        B, D, T = (4, 256, 512)
        x = jax.random.normal(k1, (B, D, T), dtype=jnp.float32)
        mask = jax.random.randint(k2, (B, T), 0, 2).astype(jnp.float32)
        lim = float(np.sqrt(6.0 / (D + D)))
        Wq = jax.random.uniform(k3, (D, D), dtype=jnp.float32, minval=-lim, maxval=lim)
        Wo = jax.random.uniform(k4, (D, D), dtype=jnp.float32, minval=-lim, maxval=lim)
        return {'x': x, 'mask': mask, 'Wq': Wq, 'Wo': Wo}
    _L0_cond_all = _L0_cond_setup()
    _L0_cond_in = {k: v for k, v in _L0_cond_all.items() if k in ('Wq', 'Wo')}
    del _L0_cond_all

    def _L1_cond_setup():
        import jax, jax.numpy as jnp
        import numpy as np
        import math
        D_MODEL = 256
        NUM_HEAD = 16
        NEG_INF = -1e+30
        key = jax.random.key(seed)
        k_x, k_m, k_q, k_k, k_v = jax.random.split(key, 5)
        B, C, T = (4, D_MODEL, 512)
        x = jax.random.normal(k_x, (B, C, T), dtype=jnp.float32)
        mask = (jax.random.uniform(k_m, (B, T)) < 0.9).astype(jnp.float32)
        limit = math.sqrt(6.0 / (C + C))
        Wq = jax.random.uniform(k_q, (C, C), minval=-limit, maxval=limit, dtype=jnp.float32)
        Wk = jax.random.uniform(k_k, (C, C), minval=-limit, maxval=limit, dtype=jnp.float32)
        Wv = jax.random.uniform(k_v, (C, C), minval=-limit, maxval=limit, dtype=jnp.float32)
        b = jnp.zeros((1,), dtype=jnp.float32)
        return {'x': x, 'mask': mask, 'Wq': Wq, 'Wk': Wk, 'Wv': Wv, 'b': b}
    _L1_cond_all = _L1_cond_setup()
    _L1_cond_in = {k: v for k, v in _L1_cond_all.items() if k in ('Wq', 'Wk', 'Wv', 'b')}
    del _L1_cond_all
    return {'x': x, 'cond_2048': cond_2048, 'L0_cond_Wq': _L0_cond_in['Wq'], 'L0_cond_Wo': _L0_cond_in['Wo'], 'L1_cond_Wq': _L1_cond_in['Wq'], 'L1_cond_Wk': _L1_cond_in['Wk'], 'L1_cond_Wv': _L1_cond_in['Wv'], 'L1_cond_b': _L1_cond_in['b']}

def reference(x, cond_2048, L0_cond_Wq, L0_cond_Wo, L1_cond_Wq, L1_cond_Wk, L1_cond_Wv, L1_cond_b):
    import jax
    import jax.numpy as jnp

    def _L0_cond_ref(x, mask, Wq, Wo):
        import jax, jax.numpy as jnp
        import numpy as np
        NH = 8
        NEG = -1e+30
        B, D, T = x.shape
        dk = D // NH
        scale = 1.0 / jnp.sqrt(jnp.asarray(dk, x.dtype))
        xt = jnp.transpose(x, (0, 2, 1))
        q = xt @ Wq.T
        qh = q.reshape(B, T, NH, dk).transpose(0, 2, 1, 3)
        scores = scale * jnp.einsum('bhqd,bhkd->bhqk', qh, qh)
        cmask = mask[:, None, None, :]
        rmask = mask[:, None, :, None]
        logits = (scores * cmask + (1.0 - cmask) * NEG) * rmask
        attn = jax.nn.softmax(logits, axis=-1)
        ctx = jnp.einsum('bhqk,bhkd->bhqd', attn, qh)
        ctx = ctx.transpose(0, 2, 1, 3).reshape(B, T, D)
        out = ctx @ Wo.T
        return jnp.transpose(out, (0, 2, 1))

    def _L1_cond_ref(x, mask, Wq, Wk, Wv, b):
        import jax, jax.numpy as jnp
        import numpy as np
        import math
        D_MODEL = 256
        NUM_HEAD = 16
        NEG_INF = -1e+30
        B, C, T = x.shape
        H = NUM_HEAD
        Dh = C // H

        def proj(W):
            y = jnp.einsum('oc,bct->bto', W, x)
            return y.reshape(B, T, H, Dh).transpose(0, 2, 1, 3)
        Q, K, V = (proj(Wq), proj(Wk), proj(Wv))
        att = jnp.einsum('bhqd,bhkd->bhqk', Q, K) * (1.0 / math.sqrt(Dh))
        att = att + b[0]
        m = mask[:, None, None, :]
        att = att * m + (1.0 - m) * NEG_INF
        att = jax.nn.softmax(att, axis=-1)
        y = jnp.einsum('bhqk,bhkd->bhqd', att, V)
        y = y.transpose(0, 2, 1, 3).reshape(B, T, C)
        return y.transpose(0, 2, 1)
    x = x + _L0_cond_ref(x, cond_2048, L0_cond_Wq, L0_cond_Wo)
    x = x + _L1_cond_ref(x, cond_2048, L1_cond_Wq, L1_cond_Wk, L1_cond_Wv, L1_cond_b)
    return x

_drawn_inputs = setup_inputs


def setup_inputs(seed=0):
    import zlib

    import numpy as np

    out = dict(_drawn_inputs(seed))
    spreads = {}
    factors = {}
    for name, (base, spread) in spreads.items():
        noise = np.random.default_rng([zlib.crc32(name.encode()), seed]).standard_normal(out[name].shape)
        drawn = base * np.exp(spread * noise) if base else spread * noise
        out[name] = jnp.asarray(drawn.astype(out[name].dtype))
    for name, factor in factors.items():
        out[name] = (out[name] * factor).astype(out[name].dtype)
    return out
```

```python
from contextlib import ExitStack

import concourse.bass as bass
from concourse import mybir

F32 = mybir.dt.float32
F32R = mybir.dt.float32r
ALU = mybir.AluOpType
ACT = mybir.ActivationFunctionType
AX = mybir.AxisListType

P = 128
GROUP = 4
NEG = -1e30
PART = 32
MASK_ROW = 3 * PART
MAX_ROW = MASK_ROW + 2


def due(count):
    return not (isinstance(count, int) and count <= 0)


def build_layer(nc, layer, x_in, mask, bias, w_in, w_out, unit_rows, ident_in, x_out):
    B, D, T = x_in.shape
    C = D // P
    first = layer == 0
    H = 8 if first else 16
    DK = D // H
    G = H // GROUP
    KC = T // P
    QC = T // P
    RSCALE = float(DK) ** 0.5
    SCALE = 1.0 / RSCALE
    KINDS = ["Q"] if first else ["Q", "K"]
    MASKED = "Q" if first else "K"
    SOURCE = {"Q": "Q", "K": "K", "V": "Q" if first else "V"}
    QSLOTS = D // PART
    ROWS = MAX_ROW + (2 if first else 4)
    STEPS = G * KC
    HALF = GROUP * (QC // 2)
    order = ["V", "O", "Q"] if first else ["V", "Q", "K"]
    UNITS = {s: (order[s // 2], s % 2) for s in range(6)}
    RAW_LOADS = 3 + (3 if first else 6) + 1 + (1 if first else 0)
    name = lambda s: f"l{layer}_{s}"

    with ExitStack() as ctx:
        def sb(n, shape, dt=F32):
            return ctx.enter_context(nc.sbuf_tensor(name(n), shape, dt))

        def ps(n):
            return ctx.enter_context(nc.psum_tensor(name(n), [P, 512], F32))

        def sem(n):
            return ctx.enter_context(nc.semaphore(name(n)))

        def dram(n, shape):
            return nc.dram_tensor(name(n), shape, F32, kind="Internal").ap()

        parts_dram = {(k, p): dram(f"{k}{p}_parts", (B, D, T)) for k in KINDS for p in ("hi", "lo")}
        mask_rows = dram("mask_rows", (2, B, T))
        keep_rows = dram("keep_rows", (B, T))
        max_rows = dram("max_rows", (B * G, 32, P))

        q_tile = sb("q_tile", [P, 2, QSLOTS, T], F32R)
        k_tile = sb("k_tile", [P, 2, H, T], F32R)
        probs = sb("probs", [P, 2, GROUP, T])
        v_tile = sb("v_tile", [P, 2, KC, H, 32])
        x_tile = sb("x_tile", [P, C, T])
        x_hi = sb("x_hi", [P, 2, C, T], F32R)
        x_lo = sb("x_lo", [P, 2, C, T], F32R)
        mask_b = sb("mask_b", [P, T])
        raw = {k: sb(f"raw_{k}", [P, C, T]) for k in KINDS}
        hi = {k: sb(f"hi_{k}", [P, C, T], F32R) for k in KINDS}
        lo = {k: sb(f"lo_{k}", [P, C, T], F32R) for k in KINDS}
        w_raw = sb("w_raw", [P, C, D])
        w_hi = {k: sb(f"w_hi_{k}", [P, C, D], F32R) for k in w_in}
        w_lo = {k: sb(f"w_lo_{k}", [P, C, D], F32R) for k in w_in}
        ident = sb("ident", [P, P])
        one_col = sb("one_col", [P, 1])
        row_max = sb("row_max", [P, 2, GROUP * QC])
        max_split = sb("max_split", [P, 2 * GROUP * QC])
        max_t = sb("max_t", [2 * GROUP * QC, P])
        keep, mrow, mrow_hi, mrow_lo = (probs[0:B, 0, j] for j in range(4))
        bias_col = sb("bias_col", [B, 2])
        if first:
            w_o = sb("w_o", [P, C, D])
            ones = sb("ones", [P, 32])
            inv_sum = sb("inv_sum", [P, T])
            context = sb("context", [P, C, T])
            resid = sb("resid", [P, C, T])
            x1 = sb("x1", [P, C, T])
        else:
            unit = sb("unit", [P, 2])
            ctx_sb = sb("ctx_sb", [P, T])
            sums_sb = sb("sums_sb", [P, T])
            y_tile = sb("y_tile", [P, G, T])

        s_bank = [ps("s0"), ps("s1")]
        st_bank = [ps("st0"), ps("st1")]
        ctx_bank = [ps("ctx0"), ps("ctx1")]
        proj_bank = ps("proj")
        maxt_bank = ps("maxt")

        w_loaded = sem("w_loaded")
        w_taken = sem("w_taken")
        w_half = sem("w_half")
        w_split = sem("w_split")
        consts_loaded = sem("consts_loaded")
        tiles_set = sem("tiles_set")
        v_set = sem("v_set")
        y_set = sem("y_set")
        q_set = sem("q_set")
        one_set = sem("one_set")
        mrow_step = sem("mrow_step")
        mrow_stored = sem("mrow_stored")
        x_loaded = sem("x_loaded")
        mask_loaded = sem("mask_loaded")
        x_hi_done = sem("x_hi_done")
        x_split = sem("x_split")
        proj_full = {k: sem(f"proj_full_{k}") for k in ("V", "Q", "K", "O")}
        proj_read = {k: sem(f"proj_read_{k}") for k in ("V", "Q", "K", "O")}
        masked = sem("masked")
        hi_done = {k: sem(f"hi_done_{k}") for k in KINDS}
        lo_done = {k: sem(f"lo_done_{k}") for k in KINDS}
        parts_stored = {k: sem(f"parts_stored_{k}") for k in KINDS}
        stack_loaded = sem("stack_loaded")
        s_full = sem("s_full")
        max_done = sem("max_done")
        max_neg = sem("max_neg")
        max_split_done = sem("max_split_done")
        maxt_full = sem("maxt_full")
        maxt_read = sem("maxt_read")
        maxt_stored = sem("maxt_stored")
        maxt_loaded = sem("maxt_loaded")
        st_full = sem("st_full")
        exp_done = sem("exp_done")
        pv_done = sem("pv_done")
        ctx_read = sem("ctx_read")
        inv_done = sem("inv_done")
        sums_done = sem("sums_done")
        scaled = sem("scaled")
        resid_loaded = sem("resid_loaded")
        added = sem("added")
        out_stored = sem("out_stored")

        RESID_LOADS = 1 if first else GROUP
        OUT_STORES = 1 if first else GROUP

        def batches(eng, emit):
            emit(0, 0)
            emit(1, 1)
            with eng.Fori(1, B // 2 - 1) as pair:
                emit(pair * 2, 0)
                emit(pair * 2 + 1, 1)
            emit(B - 2, 0)
            emit(B - 1, 1)

        def exists(n, ahead):
            return not isinstance(n, int) or n + ahead < B

        def max_units(n, par, g):
            for ahead, chunks in ((1, range(QC // 2, QC)), (2, range(QC // 2))):
                m, mp, mg = (n, par, g + ahead) if g + ahead < G else (n + 1, 1 - par, g + ahead - G)
                if g + ahead >= G and not exists(n, 1):
                    continue
                for qc in chunks:
                    for j in range(GROUP):
                        yield m, mp, mg, qc, j

        def first_units():
            for g, chunks in ((0, range(QC)), (1, range(QC // 2))):
                for qc in chunks:
                    for j in range(GROUP):
                        yield 0, 0, g, qc, j

        def units_of_step(n, par, g, c):
            per = GROUP * QC
            return list(max_units(n, par, g))[per * c // KC:per * (c + 1) // KC]

        def completes(u):
            return u[3] == QC - 1 and u[4] == GROUP - 1

        def unit_ahead(kind):
            return {"V": 1, "Q": 2, "K": 2, "O": -1}[kind]

        def unit_of_step(n, s):
            if s not in UNITS:
                return None
            kind, half = UNITS[s]
            m = n + unit_ahead(kind)
            if isinstance(m, int) and not 0 <= m < B:
                return None
            return kind, half, m

        PROLOGUE = [(k, h, m) for m in (0, 1) for k in KINDS for h in range(2)] + [("V", h, 0) for h in range(2)]

        def q_slot(h):
            return h if first else h // 2

        block = ctx.enter_context(nc.Block())

        @block.sync
        def _(sp):
            def load_x(n, par):
                sp.dma_start(x_tile[:, :], x_in[n].rearrange("(c p) t -> p c t", p=P)).then_inc(x_loaded, 16)

            def load_stack(n, par):
                if due(n - 1):
                    sp.wait_ge(pv_done, STEPS * (n - 1))
                sp.dma_start(k_tile[MASK_ROW:MASK_ROW + 2, par].bitcast(F32),
                             mask_rows[:, n].unsqueeze(1).broadcast_to([2, H, T])).then_inc(stack_loaded, 16)
                for k in KINDS:
                    sp.wait_ge(parts_stored[k], 32 * (n + 1))
                for row, part in enumerate(("hi", "lo", "hi")):
                    sp.dma_start(q_tile[row * PART:(row + 1) * PART, par].bitcast(F32),
                                 parts_dram["Q", part][n].rearrange("(s r) t -> r s t", r=PART)).then_inc(stack_loaded, 16)
                for row, part in enumerate(("hi", "hi", "lo")):
                    if first:
                        sp.dma_start(k_tile[row * PART:(row + 1) * PART, par].bitcast(F32),
                                     parts_dram["Q", part][n].rearrange("(s r) t -> r s t", r=PART)).then_inc(stack_loaded, 16)
                    else:
                        src = parts_dram["K", part][n].rearrange("(s two r) t -> two r s t", two=2, r=DK)
                        dst = k_tile[:, par].bitcast(F32).rearrange("p (s two) t -> p two s t", two=2)
                        for odd in range(2):
                            at = row * PART + odd * DK
                            sp.dma_start(dst[at:at + DK, odd], src[odd]).then_inc(stack_loaded, 16)
                if first:
                    sp.dma_start(q_tile[MASK_ROW:MASK_ROW + 2, par].bitcast(F32),
                                 keep_rows[n].unsqueeze(0).unsqueeze(0).broadcast_to([2, H, T])).then_inc(stack_loaded, 16)

            def load_mask(n):
                sp.dma_start(mask_b[:, :], mask[n].unsqueeze(0).broadcast_to([P, T])).then_inc(mask_loaded, 16)

            def store_parts(k, n):
                sp.wait_ge(hi_done[k], 2 * (n + 1))
                sp.dma_start(parts_dram[k, "hi"][n].rearrange("(c p) t -> p c t", p=P), hi[k][:].bitcast(F32)).then_inc(parts_stored[k], 16)
                sp.wait_ge(lo_done[k], 2 * (n + 1))
                sp.dma_start(parts_dram[k, "lo"][n].rearrange("(c p) t -> p c t", p=P), lo[k][:].bitcast(F32)).then_inc(parts_stored[k], 16)

            def move_max(m, mp, g):
                gg = m * G + g
                sp.wait_ge(maxt_read, gg + 1)
                sp.dma_start(max_rows[gg], max_t[:, :]).then_inc(maxt_stored, 16)
                sp.wait_ge(maxt_stored, 16 * (gg + 1))
                if first:
                    dst = q_tile[MAX_ROW:ROWS, mp, g * GROUP:(g + 1) * GROUP]
                    src = max_rows[gg].rearrange("(hl j c) p -> hl j (c p)", hl=2, j=GROUP)
                else:
                    dst = q_tile[MAX_ROW:ROWS, mp, g * 2:(g + 1) * 2]
                    src = max_rows[gg].rearrange("(hl j c) p -> hl j (c p)", hl=4, j=2)
                sp.dma_start(dst.bitcast(F32), src).then_inc(maxt_loaded, 16)

            def load_resid(n):
                if first:
                    if due(n):
                        sp.wait_ge(proj_read["O"], 2 * n)
                    sp.dma_start(resid[:, :], x_in[n].rearrange("(c p) t -> p c t", p=P)).then_inc(resid_loaded, 16)
                else:
                    if due(n):
                        sp.wait_ge(out_stored, 16 * OUT_STORES * n)
                    else:
                        sp.wait_ge(y_set, 1)
                    src = x_in[n].rearrange("(g j r) t -> j r g t", j=GROUP, r=DK)
                    for j in range(GROUP):
                        sp.dma_start(y_tile[32 * j:32 * j + DK], src[j]).then_inc(resid_loaded, 16)

            def store_out(n):
                if first:
                    sp.wait_ge(proj_read["O"], 2 * (n + 1))
                    sp.dma_start(x_out[n].rearrange("(c p) t -> p c t", p=P), x1[:, :]).then_inc(out_stored, 16)
                else:
                    sp.wait_ge(added, G * (n + 1))
                    dst = x_out[n].rearrange("(g j r) t -> j r g t", j=GROUP, r=DK)
                    for j in range(GROUP):
                        sp.dma_start(dst[j], y_tile[32 * j:32 * j + DK]).then_inc(out_stored, 16)

            sp.dma_start(keep[:, :], mask).then_inc(consts_loaded, 16)
            sp.dma_start(bias_col[:, 0:1], bias.unsqueeze(0).broadcast_to([B, 1])).then_inc(consts_loaded, 16)
            sp.dma_start(ident[:, :], ident_in).then_inc(consts_loaded, 16)
            if first:
                sp.dma_start(w_o[:, :], w_out.rearrange("(c p) o -> p c o", p=P)).then_inc(consts_loaded, 16)
            else:
                sp.dma_start(unit[96:128, :], unit_rows).then_inc(consts_loaded, 16)
            sp.dma_start(keep_rows, mask).then_inc(consts_loaded, 16)
            load_x(0, 0)
            load_mask(0)
            for n, k in enumerate(w_in):
                if n:
                    sp.wait_ge(w_split, n)
                sp.dma_start(w_raw[:, :], w_in[k].rearrange("(c p) o -> p c o", p=P)).then_inc(w_loaded, 16)
            sp.wait_ge(x_split, 1)
            load_x(1, 1)
            sp.wait_ge(mrow_step, 4)
            sp.dma_start(mask_rows[0], mrow_hi[:, :]).then_inc(mrow_stored, 16)
            sp.dma_start(mask_rows[1], mrow_lo[:, :]).then_inc(mrow_stored, 16)
            for k in KINDS:
                store_parts(k, 0)
            sp.wait_ge(lo_done[MASKED], 2)
            load_mask(1)
            for k in KINDS:
                store_parts(k, 1)
            sp.wait_ge(mrow_stored, 32)
            sp.wait_ge(consts_loaded, 16 * 5)
            sp.wait_ge(tiles_set, 2)
            if not first:
                sp.wait_ge(q_set, 1)
            load_stack(0, 0)
            move_max(0, 0, 0)

            def batch(n, par):
                if exists(n, 1):
                    load_stack(n + 1, 1 - par)
                if exists(n, 2):
                    sp.wait_ge(x_split, n + 2)
                    load_x(n + 2, par)
                    sp.wait_ge(lo_done[MASKED], 2 * (n + 2))
                    load_mask(n + 2)
                for g in range(G):
                    units = [u for u in max_units(n, par, g) if completes(u)]
                    if g == 0 and due(n):
                        if first:
                            load_resid(n - 1)
                    for m, mp, mg, _, _ in units:
                        move_max(m, mp, mg)
                    if g == 0 and due(n):
                        store_out(n - 1)
                    if g == 0 and not first:
                        load_resid(n)
                    for k in KINDS:
                        last = max(s for s in UNITS if UNITS[s][0] == k)
                        if exists(n, 2) and last // KC == g:
                            store_parts(k, n + 2)

            batches(sp, batch)
            if first:
                load_resid(B - 1)
            store_out(B - 1)
            sp.wait_ge(out_stored, 16 * OUT_STORES * B)

        @block.gpsimd
        def _(pool):
            pool.memset(one_col[:, :], 1.0).then_inc(one_set, 1)
            pool.wait_ge(one_set, 1)
            if first:
                pool.memset(ones[:, :], 1.0).then_inc(one_set, 1)
                pool.wait_ge(one_set, 2)
                pool.memset(q_tile[96:128].bitcast(F32), 1.0).then_inc(tiles_set, 1)
                pool.memset(k_tile[96:128].bitcast(F32), 1.0).then_inc(tiles_set, 1)
                pool.wait_ge(tiles_set, 2)
            else:
                pool.memset(v_tile[:, :], 1.0).then_inc(v_set, 1)
                pool.memset(y_tile[:, :], 0.0).then_inc(y_set, 1)
                pool.wait_ge(v_set, 1)
                pool.wait_ge(y_set, 1)
                pool.memset(q_tile[96:128].bitcast(F32), 1.0).then_inc(q_set, 1)
                pool.wait_ge(q_set, 1)

            def split_x(n, par):
                pool.wait_ge(x_loaded, 16 * (n + 1))
                if due(n - 1):
                    pool.wait_ge(proj_full["V"], 2 * (n - 1))
                    pool.wait_ge(x_split, n - 1)
                pool.tensor_tensor(x_hi[:, par], x_tile[:, :], one_col[:, :].unsqueeze(2).broadcast_to([P, C, T]), ALU.mult).then_inc(x_hi_done, 1)
                pool.wait_ge(x_hi_done, n + 1)
                pool.tensor_tensor(x_lo[:, par], x_tile[:, :], x_hi[:, par].bitcast(F32), ALU.subtract).then_inc(x_split, 1)

            def split_unit(k, half, n):
                if k == MASKED:
                    pool.wait_ge(mask_loaded, 16 * (n + 1))
                    pool.wait_ge(proj_read[k], 2 * n + half + 1)
                    pool.tensor_tensor(raw[k][:, half], raw[k][:, half], mask_b[:, :], ALU.mult).then_inc(masked, 1)
                    pool.wait_ge(masked, 2 * n + half + 1)
                pool.wait_ge(hi_done[k], 2 * n + half + 1)
                if due(n):
                    pool.wait_ge(parts_stored[k], 32 * n)
                pool.tensor_tensor(lo[k][:, half], raw[k][:, half], hi[k][:, half].bitcast(F32), ALU.subtract).then_inc(lo_done[k], 1)

            def add_resid(n, g):
                pool.wait_ge(inv_done, n * G + g + 1)
                pool.tensor_tensor(ctx_sb[:, :], ctx_sb[:, :], sums_sb[:, :], ALU.mult).then_inc(scaled, 1)
                pool.wait_ge(scaled, n * G + g + 1)
                pool.wait_ge(resid_loaded, 16 * RESID_LOADS * (n + 1))
                pool.tensor_tensor(y_tile[:, g], ctx_sb[:, :], y_tile[:, g], ALU.add).then_inc(added, 1)

            split_x(0, 0)
            for k in KINDS:
                for half in range(2):
                    split_unit(k, half, 0)
            split_x(1, 1)
            for k in KINDS:
                for half in range(2):
                    split_unit(k, half, 1)

            def batch(n, par):
                if not first and due(n):
                    add_resid(n - 1, G - 1)
                if exists(n, 2):
                    split_x(n + 2, par)
                for g in range(G):
                    if not first and g > 0:
                        add_resid(n, g - 1)
                    for c in range(KC):
                        unit_here = unit_of_step(n, g * KC + c)
                        if unit_here and unit_here[0] in KINDS:
                            split_unit(*unit_here)

            batches(pool, batch)
            if not first:
                add_resid(B - 1, G - 1)

        @block.scalar
        def _(act):
            def read_unit(kind, half, n):
                act.wait_ge(proj_full[kind], 2 * n + half + 1)
                if due(n):
                    act.wait_ge(lo_done[kind], 2 * n)
                act.activation(raw[kind][:, half], proj_bank[:, :], ACT.Copy).then_inc(proj_read[kind], 1)

            def read_v(half, n, par):
                act.wait_ge(proj_full["V"], 2 * n + half + 1)
                if due(n - 1):
                    act.wait_ge(pv_done, STEPS * (n - 1))
                act.activation(v_tile[:, par, 2 * half:2 * half + 2, :, 0:DK],
                               proj_bank[:, :].rearrange("p (c h d) -> p c h d", c=2, h=H), ACT.Copy).then_inc(proj_read["V"], 1)

            def take_hi(kind, half, n):
                if kind == MASKED:
                    act.wait_ge(masked, 2 * n + half + 1)
                else:
                    act.wait_ge(proj_read[kind], 2 * n + half + 1)
                if due(n):
                    act.wait_ge(parts_stored[kind], 32 * n)
                act.activation(hi[kind][:, half], raw[kind][:, half], ACT.Copy).then_inc(hi_done[kind], 1)

            def read_max(m, g):
                gg = m * G + g
                act.wait_ge(maxt_full, gg + 1)
                if due(gg):
                    act.wait_ge(maxt_stored, 16 * gg)
                act.activation(max_t[:, :], maxt_bank[0:2 * GROUP * QC, 0:P], ACT.Copy).then_inc(maxt_read, 1)

            def read_context(gg, par):
                act.wait_ge(pv_done, KC * (gg + 1))
                if due(gg):
                    act.wait_ge(added, gg)
                act.activation(ctx_sb[:, :], ctx_bank[par][:, :], ACT.Copy).then_inc(ctx_read, 1)

            if not first:
                act.wait_ge(v_set, 1)
            for kind, half, n in PROLOGUE:
                if kind == "V":
                    read_v(half, n, 0)
                else:
                    read_unit(kind, half, n)
                    take_hi(kind, half, n)
            read_max(0, 0)

            def batch(n, par):
                late = None
                for g in range(G):
                    done = [u for u in max_units(n, par, g) if completes(u)]
                    for c in range(KC):
                        step = n * STEPS + g * KC + c
                        for j in range(GROUP):
                            act.wait_ge(st_full, GROUP * step + j + 1)
                            if j == 0 and due(step - 1):
                                act.wait_ge(pv_done, step - 1)
                            act.activation(probs[:, (g * KC + c) % 2, j], st_bank[j % 2][:, :], ACT.Exp, scale=SCALE).then_inc(exp_done, 1)
                        if late:
                            take_hi(*late)
                            late = None
                        if not first and c == 0 and due(n * G + g):
                            read_context(n * G + g - 1, (g - 1) % 2)
                        unit_here = unit_of_step(n, g * KC + c)
                        if unit_here and unit_here[0] == "V":
                            read_v(unit_here[1], unit_here[2], 1 - par)
                        elif unit_here and unit_here[0] in KINDS:
                            read_unit(*unit_here)
                            late = unit_here
                        if c == KC // 2 and done:
                            read_max(done[0][0], done[0][2])
                if late:
                    take_hi(*late)

            batches(act, batch)
            if not first:
                read_context(B * G - 1, (G - 1) % 2)

        @block.vector
        def _(dve):
            for n, k in enumerate(w_in):
                dve.wait_ge(w_loaded, 16 * (n + 1))
                dve.tensor_copy(w_hi[k][:, :], w_raw[:, :]).then_inc(w_half, 1)
                dve.wait_ge(w_half, n + 1)
                dve.tensor_tensor(w_lo[k][:, :], w_raw[:, :], w_hi[k][:, :].bitcast(F32), ALU.subtract).then_inc(w_split, 1)
            dve.wait_ge(consts_loaded, 16 * 5)
            dve.tensor_scalar(bias_col[:, 1:2], bias_col[:, 0:1], 0.0 if first else RSCALE, None, ALU.mult).then_inc(mrow_step, 1)
            dve.tensor_scalar(mrow[:, :], keep[:, :], -NEG * RSCALE, NEG * RSCALE, ALU.mult, ALU.add).then_inc(mrow_step, 1)
            dve.wait_ge(mrow_step, 2)
            if not first:
                dve.scalar_tensor_tensor(out=mrow[:, :], in0=keep[:, :], scalar=bias_col[:, 1:2], in1=mrow[:, :],
                                         op0=ALU.mult, op1=ALU.add).then_inc(w_taken, 1)
                dve.wait_ge(w_taken, 1)
            dve.tensor_copy(mrow_hi[:, :].bitcast(F32R), mrow[:, :]).then_inc(mrow_step, 1)
            dve.wait_ge(mrow_step, 3)
            dve.tensor_tensor(mrow_lo[:, :].bitcast(F32R), mrow[:, :], mrow_hi[:, :], ALU.subtract).then_inc(mrow_step, 1)
            if not first:
                dve.memset(k_tile[0:96].bitcast(F32), 0.0).then_inc(tiles_set, 1)
                for odd in range(2):
                    view = k_tile[96:128].rearrange("p q (s two) t -> p (q s) two t", two=2)
                    last = dve.tensor_copy(view[:, :, odd], unit[96:128, odd:odd + 1].unsqueeze(2).broadcast_to([32, H, T]))
                last.then_inc(tiles_set, 1)

            def maximum(m, g, qc, j):
                n = ((m * G + g) * QC + qc) * GROUP + j
                if qc == 0 and j == 0 and due(m * G + g - 1):
                    dve.wait_ge(max_split_done, m * G + g - 1)
                dve.wait_ge(s_full, n + 1)
                col = j * QC + qc if first else (j % 2) * 2 * QC + (j // 2) * QC + qc
                dve.tensor_reduce(row_max[:, g % 2, col:col + 1], s_bank[j % 2][:, :], AX.X, ALU.max).then_inc(max_done, 1)

            def split_max(m, g):
                gg = m * G + g
                dve.wait_ge(max_done, GROUP * QC * (gg + 1))
                if due(gg):
                    dve.wait_ge(maxt_full, gg)
                outer = 1 if first else 2
                view = max_split[:, :].rearrange("p (o hl r) -> p hl o r", o=outer, hl=2)
                src = row_max[:, g % 2].rearrange("p (o r) -> p o r", o=outer)
                dve.tensor_scalar(view[:, 0].bitcast(F32R), src, -1.0, None, ALU.mult).then_inc(max_neg, 1)
                dve.wait_ge(max_neg, gg + 1)
                dve.scalar_tensor_tensor(out=view[:, 1].bitcast(F32R), in0=src, scalar=-1.0, in1=view[:, 0],
                                         op0=ALU.mult, op1=ALU.subtract).then_inc(max_split_done, 1)

            def scale_context(n, g):
                gg = n * G + g
                dve.wait_ge(pv_done, KC * (gg + 1))
                if due(gg):
                    dve.wait_ge(ctx_read, gg)
                dve.reciprocal(inv_sum[:, :], ctx_bank[1][:, :]).then_inc(inv_done, 1)
                dve.wait_ge(inv_done, gg + 1)
                if due(n):
                    dve.wait_ge(proj_full["O"], 2 * n)
                dve.tensor_tensor(context[:, g], ctx_bank[0][:, :], inv_sum[:, :], ALU.mult).then_inc(ctx_read, 1)

            def invert_sums(gg):
                dve.wait_ge(ctx_read, gg + 1)
                if due(gg):
                    dve.wait_ge(scaled, gg)
                dve.reciprocal(sums_sb[:, :], ctx_sb[:, :])
                dve.drain()
                dve.stream_shuffle(sums_sb[:, :], sums_sb[:, :], [i % DK + DK for i in range(32)]).then_inc(inv_done, 1)

            def add_resid(half, n):
                dve.wait_ge(resid_loaded, 16 * (n + 1))
                dve.wait_ge(proj_full["O"], 2 * n + half + 1)
                if due(n):
                    dve.wait_ge(out_stored, 16 * n)
                dve.tensor_tensor(x1[:, half], proj_bank[:, :], resid[:, half], ALU.add).then_inc(proj_read["O"], 1)

            for m, mp, g, qc, j in first_units():
                maximum(m, g, qc, j)
                if completes((m, mp, g, qc, j)):
                    split_max(m, g)

            def batch(n, par):
                for g in range(G):
                    for c in range(KC):
                        for u in units_of_step(n, par, g, c):
                            maximum(u[0], *u[2:])
                            if completes(u):
                                split_max(u[0], u[2])
                        if first and c == 0:
                            if g > 0:
                                scale_context(n, g - 1)
                            elif due(n):
                                scale_context(n - 1, G - 1)
                        if not first and c == 1 and due(n * G + g):
                            invert_sums(n * G + g - 1)
                        unit_here = unit_of_step(n, g * KC + c)
                        if unit_here and unit_here[0] == "O":
                            add_resid(*unit_here[1:])

            batches(dve, batch)
            if first:
                scale_context(B - 1, G - 1)
                for half in range(2):
                    add_resid(half, B - 1)
            else:
                invert_sums(B * G - 1)

        @block.tensor
        def _(pe):
            tenant = [None]

            def project(kind, half, n, par):
                if tenant[0]:
                    pe.wait_ge(*tenant[0])
                if kind == "O":
                    pe.wait_ge(ctx_read, G * (n + 1))
                    for c in range(C):
                        last = pe.matmul(proj_bank[:, :], w_o[:, c, half * P:(half + 1) * P], context[:, c], start=c == 0, stop=c == C - 1)
                    last.then_inc(proj_full["O"], 1)
                else:
                    pe.wait_ge(x_split, n + 1)
                    w = SOURCE[kind]
                    pairs = [(x_hi, w_hi[w]), (x_lo, w_hi[w]), (x_hi, w_lo[w])]
                    if kind == "V":
                        for t in range(2):
                            token = (2 * half + t) * P
                            for i, (c, (x, wp)) in enumerate((c, pr) for c in range(C) for pr in pairs):
                                last = pe.matmul(proj_bank[:, t * D:(t + 1) * D], x[:, par, c, token:token + P], wp[:, c], start=i == 0, stop=i == 3 * C - 1)
                    else:
                        for i, (c, (x, wp)) in enumerate((c, pr) for c in range(C) for pr in pairs):
                            last = pe.matmul(proj_bank[:, :], wp[:, c, half * P:(half + 1) * P], x[:, par, c], start=i == 0, stop=i == 3 * C - 1)
                    last.then_inc(proj_full[kind], 1)
                tenant[0] = (proj_read[kind], 2 * n + half + 1)

            def scores(m, mp, g, qc, j):
                n = ((m * G + g) * QC + qc) * GROUP + j
                h = g * GROUP + j
                if g == 0 and qc == 0 and j == 0:
                    pe.wait_ge(stack_loaded, 16 * RAW_LOADS * (m + 1))
                if due(n - 1):
                    pe.wait_ge(max_done, n - 1)
                pe.matmul(s_bank[j % 2][:, :], q_tile[0:MAX_ROW, mp, q_slot(h), qc * P:(qc + 1) * P],
                          k_tile[0:MAX_ROW, mp, h], start=True, stop=True).then_inc(s_full, 1)

            def transpose_max(m, g):
                gg = m * G + g
                pe.wait_ge(max_split_done, gg + 1)
                if due(gg):
                    pe.wait_ge(maxt_read, gg)
                pe.matmul(maxt_bank[0:2 * GROUP * QC, 0:P], max_split[:, :], ident[:, :], start=True, stop=True).then_inc(maxt_full, 1)

            def scores_t(n, par, g, c, j):
                unit_no = GROUP * (n * STEPS + g * KC + c) + j
                h = g * GROUP + j
                if c == 0 and j == 0:
                    pe.wait_ge(maxt_loaded, 16 * (n * G + g + 1))
                if due(unit_no - 1):
                    pe.wait_ge(exp_done, unit_no - 1)
                pe.matmul(st_bank[j % 2][:, :], k_tile[0:ROWS, par, h, c * P:(c + 1) * P],
                          q_tile[0:ROWS, par, q_slot(h)], start=True, stop=True).then_inc(st_full, 1)

            def attend(n, par, g, c):
                step = n * STEPS + g * KC + c
                gg = n * G + g
                pe.wait_ge(exp_done, GROUP * (step + 1))
                if c == 0:
                    pe.wait_ge(proj_read["V"], 2 * (n + 1))
                    if due(gg if first else gg - 1):
                        pe.wait_ge(ctx_read, gg if first else gg - 1)
                bank = ctx_bank[0 if first else g % 2]
                for j in range(GROUP):
                    last = pe.matmul(bank[32 * j:32 * j + 32, :], v_tile[:, par, c, g * GROUP + j],
                                     probs[:, (g * KC + c) % 2, j], start=c == 0, stop=c == KC - 1)
                if first:
                    for j in range(GROUP):
                        last = pe.matmul(ctx_bank[1][32 * j:32 * j + 32, :], ones[:, :],
                                         probs[:, (g * KC + c) % 2, j], start=c == 0, stop=c == KC - 1)
                last.then_inc(pv_done, 1)

            pe.wait_ge(w_split, len(w_in))
            pe.wait_ge(consts_loaded, 16 * 5)
            pe.wait_ge(tiles_set, 2)
            if not first:
                pe.wait_ge(q_set, 1)
            for kind, half, n in PROLOGUE:
                project(kind, half, n, n)
            for u in first_units():
                scores(*u)
                if completes(u):
                    transpose = u
            transpose_max(0, 0)

            def batch(n, par):
                if not isinstance(n, int) or n == B - 2:
                    if par == 0:
                        tenant[0] = (proj_read[KINDS[-1]], 2 * (n + 1) + 2)
                for g in range(G):
                    pending = None
                    for c in range(KC):
                        units = units_of_step(n, par, g, c)
                        for j in range(GROUP):
                            for u in units[len(units) * j // GROUP:len(units) * (j + 1) // GROUP]:
                                scores(*u)
                                if completes(u):
                                    pending = (u[0], u[2])
                            scores_t(n, par, g, c, j)
                        if c > 0:
                            attend(n, par, g, c - 1)
                        elif g > 0:
                            attend(n, par, g - 1, KC - 1)
                        elif due(n):
                            attend(n - 1, 1 - par, G - 1, KC - 1)
                        unit_here = unit_of_step(n, g * KC + c)
                        if unit_here:
                            kind, half, m = unit_here
                            project(kind, half, m, 1 - par if kind == "V" else par)
                        if c == KC // 2 and pending:
                            transpose_max(*pending)
                            pending = None

            batches(pe, batch)
            attend(B - 1, 1, G - 1, KC - 1)
            if first:
                for half in range(2):
                    project("O", half, B - 1, 0)


def build(nc, x, mask, wq0_t, wo0_t, wq1_t, wk1_t, wv1_t, bias, unit_rows, ident, out):
    x1 = nc.dram_tensor("x1_scratch", x.shape, F32, kind="Internal").ap()
    build_layer(nc, 0, x, mask, bias, {"Q": wq0_t}, wo0_t, None, ident, x1)
    build_layer(nc, 1, x1, mask, bias, {"Q": wq1_t, "K": wk1_t, "V": wv1_t}, None, unit_rows, ident, out)


def kernel(x, cond_2048, L0_cond_Wq, L0_cond_Wo, L1_cond_Wq, L1_cond_Wk, L1_cond_Wv, L1_cond_b):
    import concourse.bacc as bacc
    import numpy as np
    from concourse.bass_utils import run_bass_kernel_spmd

    unit_rows = np.zeros((32, 2), np.float32)
    unit_rows[2:4, 0] = 1.0
    unit_rows[4:6, 1] = 1.0
    arrays = {
        "x": np.ascontiguousarray(x),
        "mask": np.ascontiguousarray(cond_2048),
        "wq0_t": np.ascontiguousarray(np.transpose(L0_cond_Wq)),
        "wo0_t": np.ascontiguousarray(np.transpose(L0_cond_Wo)),
        "wq1_t": np.ascontiguousarray(np.transpose(L1_cond_Wq)),
        "wk1_t": np.ascontiguousarray(np.transpose(L1_cond_Wk)),
        "wv1_t": np.ascontiguousarray(np.transpose(L1_cond_Wv)),
        "bias": np.ascontiguousarray(L1_cond_b),
        "unit_rows": unit_rows,
        "ident": np.eye(P, dtype=np.float32),
    }
    nc = bacc.Bacc("TRN2", target_bir_lowering=False, num_devices=1)
    args = [nc.dram_tensor(f"in_{k}", a.shape, F32, kind="ExternalInput").ap() for k, a in arrays.items()]
    args.append(nc.dram_tensor("out", arrays["x"].shape, F32, kind="ExternalOutput").ap())
    build(nc, *args)
    result = run_bass_kernel_spmd(nc, [{f"in_{k}": a for k, a in arrays.items()}], core_ids=[0])
    return result.results[0]["out"]
```

```python
from contextlib import ExitStack

import concourse.bass as bass
from concourse import mybir

F32 = mybir.dt.float32
F32R = mybir.dt.float32r
ALU = mybir.AluOpType
ACT = mybir.ActivationFunctionType
AX = mybir.AxisListType

P = 128
GROUP = 4
NEG = -1e30
PART = 32
MASK_ROW = 3 * PART
MAX_ROW = MASK_ROW + 2


def due(count):
    return not (isinstance(count, int) and count <= 0)


def build_layer(nc, layer, x_in, mask, bias, w_in, w_out, unit_rows, ident_in, x_out):
    B, D, T = x_in.shape
    C = D // P
    first = layer == 0
    H = 8 if first else 16
    DK = D // H
    G = H // GROUP
    KC = T // P
    QC = T // P
    RSCALE = float(DK) ** 0.5
    SCALE = 1.0 / RSCALE
    KINDS = ["Q"] if first else ["Q", "K"]
    MASKED = "Q" if first else "K"
    SOURCE = {"Q": "Q", "K": "K", "V": "Q" if first else "V"}
    QSLOTS = D // PART
    ROWS = MAX_ROW + (2 if first else 4)
    STEPS = G * KC
    STACKS = 2
    AHEAD = 2 if first else 3
    SPLIT_STEP = 0 if first else 3
    INV_STEP = KC - 2
    if first:
        UNITS = {4: ("V", 0), 5: ("V", 1), 2: ("Q", 0), 3: ("Q", 1), STEPS - 2: ("O", 0), STEPS - 1: ("O", 1)}
    else:
        UNITS = {0: ("V", 0), 3: ("V", 1), 6: ("Q", 0), 8: ("Q", 1), 10: ("K", 0), 11: ("K", 1)}
    RAW_LOADS = 3 + (3 if first else 6) + 1 + (1 if first else 0)
    name = lambda s: f"l{layer}_{s}"

    with ExitStack() as ctx:
        def sb(n, shape, dt=F32):
            return ctx.enter_context(nc.sbuf_tensor(name(n), shape, dt))

        def ps(n):
            return ctx.enter_context(nc.psum_tensor(name(n), [P, 512], F32))

        def sem(n):
            return ctx.enter_context(nc.semaphore(name(n)))

        def dram(n, shape):
            return nc.dram_tensor(name(n), shape, F32, kind="Internal").ap()

        parts_dram = {(k, p): dram(f"{k}{p}_parts", (B, D, T)) for k in KINDS for p in ("hi", "lo")}
        mask_rows = dram("mask_rows", (2, B, T))
        keep_rows = dram("keep_rows", (B, T))
        max_rows = dram("max_rows", (B * G, 32, P))
        sum_rows = dram("sum_rows", (B * G, GROUP, T))
        inv_rows = dram("inv_rows", (B * G, GROUP, T))

        q_tile = sb("q_tile", [P, 2, QSLOTS, T], F32R)
        k_tile = sb("k_tile", [P, 2, H, T], F32R)
        probs = sb("probs", [P, 2, GROUP, T])
        v_tile = sb("v_tile", [P, 2, KC, H, 32])
        x_tile = sb("x_tile", [P, C, T])
        x_hi = sb("x_hi", [P, 2, C, T], F32R)
        x_lo = sb("x_lo", [P, 2, C, T], F32R)
        mask_b = sb("mask_b", [P, T])
        raw = {k: sb(f"raw_{k}", [P, C, T]) for k in KINDS}
        hi = {k: sb(f"hi_{k}", [P, C, T], F32R) for k in KINDS}
        lo = {k: sb(f"lo_{k}", [P, C, T], F32R) for k in KINDS}
        w_raw = {k: raw[k][:, :, 0:D] if k in raw else sb(f"w_raw_{k}", [P, C, D])[:, :] for k in w_in}
        w_hi = {k: sb(f"w_hi_{k}", [P, C, D], F32R) for k in w_in}
        w_lo = {k: sb(f"w_lo_{k}", [P, C, D], F32R) for k in w_in}
        ctx_sb = sb("ctx_sb", [P, 2, T])
        sums_flat = sb("sums_flat", [P, T // 32])
        inv_flat = sb("inv_flat", [P, T // 32])
        inv_sum = sb("inv_sum", [P, T])
        ident = sb("ident", [P, P])
        row_max = sb("row_max", [P, 2, GROUP * QC])
        max_split = sb("max_split", [P, 2 * GROUP * QC])
        max_t = sb("max_t", [2 * GROUP * QC, P])
        keep, mrow, mrow_hi, mrow_lo = (probs[0:B, 0, j] for j in range(4))
        bias_col = sb("bias_col", [B, 2])
        if first:
            w_o = sb("w_o", [P, C, D])
            ones = sb("ones", [P, 32])
            sums_sb = sb("sums_sb", [P, T])
            context = sb("context", [P, 2, C, T])
            resid = sb("resid", [P, C, T])
            x1 = sb("x1", [P, C, T])
        else:
            unit = sb("unit", [P, 2])
            y_tile = sb("y_tile", [P, G, T])

        s_bank = [ps("s0"), ps("s1")]
        st_bank = [ps("st0"), ps("st1")]
        ctx_bank = [ps("ctx0"), ps("ctx1")]
        proj_bank = ps("proj")
        maxt_bank = ps("maxt")
        unit_bank = [proj_bank, ctx_bank[0]]

        w_loaded = {k: sem(f"w_loaded_{k}") for k in w_in}
        bias_added = sem("bias_added")
        w_half = sem("w_half")
        w_split = sem("w_split")
        consts_loaded = sem("consts_loaded")
        tiles_set = sem("tiles_set")
        v_set = sem("v_set")
        y_set = sem("y_set")
        q_set = sem("q_set")
        k_set = sem("k_set")
        k_odd_set = sem("k_odd_set")
        one_set = sem("one_set")
        mrow_step = sem("mrow_step")
        mrow_stored = sem("mrow_stored")
        x_loaded = sem("x_loaded")
        mask_loaded = sem("mask_loaded")
        x_hi_done = sem("x_hi_done")
        x_split = sem("x_split")
        proj_full = {k: sem(f"proj_full_{k}") for k in ("V", "Q", "K", "O")}
        proj_read = {k: sem(f"proj_read_{k}") for k in ("V", "Q", "K", "O")}
        masked = sem("masked")
        hi_done = {k: sem(f"hi_done_{k}") for k in KINDS}
        lo_done = {k: sem(f"lo_done_{k}") for k in KINDS}
        parts_stored = {k: sem(f"parts_stored_{k}") for k in KINDS}
        stack_loaded = {(i, q): sem(f"stack{i}_{q}_loaded") for i in range(STACKS) for q in ("even", "odd")}
        s_full = sem("s_full")
        max_done = sem("max_done")
        max_neg = sem("max_neg")
        max_split_done = sem("max_split_done")
        maxt_full = sem("maxt_full")
        maxt_read = sem("maxt_read")
        maxt_stored = sem("maxt_stored")
        maxt_loaded = sem("maxt_loaded")
        st_full = sem("st_full")
        exp_done = sem("exp_done")
        pv_done = sem("pv_done")
        ctx_read = sem("ctx_read")
        inv_done = sem("inv_done")
        sums_read = sem("sums_read")
        sums_stored = sem("sums_stored")
        sums_loaded = sem("sums_loaded")
        inv_stored = sem("inv_stored")
        inv_loaded = sem("inv_loaded")
        scaled = sem("scaled")
        resid_loaded = sem("resid_loaded")
        added = sem("added")
        out_stored = sem("out_stored")

        RESID_LOADS = 1 if first else GROUP
        OUT_STORES = 1 if first else GROUP

        def batches(eng, emit):
            emit(0, 0)
            emit(1, 1)
            with eng.Fori(1, B // 2 - 1) as pair:
                emit(pair * 2, 0)
                emit(pair * 2 + 1, 1)
            emit(B - 2, 0)
            emit(B - 1, 1)

        def exists(n, ahead):
            return not isinstance(n, int) or n + ahead < B

        def max_units(n, par, g):
            for ahead, chunks in ((1, range(AHEAD, QC)), (2, range(AHEAD))):
                m, mp, mg = (n, par, g + ahead) if g + ahead < G else (n + 1, 1 - par, g + ahead - G)
                if g + ahead >= G and not exists(n, 1):
                    continue
                for qc in chunks:
                    for j in range(GROUP):
                        yield m, mp, mg, qc, j

        def first_units():
            for g, chunks in ((0, range(QC)), (1, range(AHEAD))):
                for qc in chunks:
                    for j in range(GROUP):
                        yield 0, 0, g, qc, j

        def units_of_step(n, par, g, c):
            per = GROUP * QC
            return list(max_units(n, par, g))[per * c // KC:per * (c + 1) // KC]

        def completes(u):
            return u[3] == QC - 1 and u[4] == GROUP - 1

        def unit_ahead(kind):
            return {"V": 1, "Q": 2, "K": 2, "O": -1}[kind]

        def unit_of_step(n, s):
            if s not in UNITS:
                return None
            kind, half = UNITS[s]
            m = n + unit_ahead(kind)
            if isinstance(m, int) and not 0 <= m < B:
                return None
            return kind, half, m

        PROLOGUE = [(k, h, m) for kinds, m in ((KINDS + ["V"], 0), (KINDS, 1)) for k in kinds for h in range(2)]

        def q_slot(h):
            return h if first else h // 2

        block = ctx.enter_context(nc.Block())

        @block.sync
        def _(sp):
            def load_x(n, par):
                sp.dma_start(x_tile[:, :], x_in[n].rearrange("(c p) t -> p c t", p=P)).then_inc(x_loaded, 16)

            def load_stack(n, par, part):
                qs = slice(part * QSLOTS // STACKS, (part + 1) * QSLOTS // STACKS)
                ks = slice(part * H // STACKS, (part + 1) * H // STACKS)
                loaded = stack_loaded[part, ("even", "odd")[par]]
                if due(n - 1):
                    sp.wait_ge(st_full, GROUP * (STEPS * (n - 2) + STEPS * (part + 1) // STACKS))
                sp.dma_start(k_tile[MASK_ROW:MASK_ROW + 2, par, ks].bitcast(F32),
                             mask_rows[:, n].unsqueeze(1).broadcast_to([2, H // STACKS, T])).then_inc(loaded, 16)
                for k in KINDS:
                    sp.wait_ge(parts_stored[k], 32 * (n + 1))
                for row, p in enumerate(("hi", "lo", "hi")):
                    sp.dma_start(q_tile[row * PART:(row + 1) * PART, par, qs].bitcast(F32),
                                 parts_dram["Q", p][n].rearrange("(s r) t -> r s t", r=PART)[:, qs]).then_inc(loaded, 16)
                for row, p in enumerate(("hi", "hi", "lo")):
                    if first:
                        sp.dma_start(k_tile[row * PART:(row + 1) * PART, par, ks].bitcast(F32),
                                     parts_dram["Q", p][n].rearrange("(s r) t -> r s t", r=PART)[:, ks]).then_inc(loaded, 16)
                    else:
                        src = parts_dram["K", p][n].rearrange("(s two r) t -> two r s t", two=2, r=DK)
                        dst = k_tile[:, par].bitcast(F32).rearrange("p (s two) t -> p two s t", two=2)
                        for odd in range(2):
                            at = row * PART + odd * DK
                            sp.dma_start(dst[at:at + DK, odd, qs], src[odd][:, qs]).then_inc(loaded, 16)
                if first:
                    sp.dma_start(q_tile[MASK_ROW:MASK_ROW + 2, par, qs].bitcast(F32),
                                 keep_rows[n].unsqueeze(0).unsqueeze(0).broadcast_to([2, H // STACKS, T])).then_inc(loaded, 16)

            def load_mask(n):
                sp.dma_start(mask_b[:, :], mask[n].unsqueeze(0).broadcast_to([P, T])).then_inc(mask_loaded, 16)

            def store_parts(k, n):
                sp.wait_ge(hi_done[k], 2 * (n + 1))
                sp.dma_start(parts_dram[k, "hi"][n].rearrange("(c p) t -> p c t", p=P), hi[k][:].bitcast(F32)).then_inc(parts_stored[k], 16)
                sp.wait_ge(lo_done[k], 2 * (n + 1))
                sp.dma_start(parts_dram[k, "lo"][n].rearrange("(c p) t -> p c t", p=P), lo[k][:].bitcast(F32)).then_inc(parts_stored[k], 16)

            def store_max(m, mp, g):
                gg = m * G + g
                sp.wait_ge(maxt_read, gg + 1)
                sp.dma_start(max_rows[gg], max_t[:, :]).then_inc(maxt_stored, 16)

            def load_max(m, mp, g):
                gg = m * G + g
                sp.wait_ge(maxt_stored, 16 * (gg + 1))
                if first:
                    dst = q_tile[MAX_ROW:ROWS, mp, g * GROUP:(g + 1) * GROUP]
                    src = max_rows[gg].rearrange("(hl j c) p -> hl j (c p)", hl=2, j=GROUP)
                else:
                    dst = q_tile[MAX_ROW:ROWS, mp, g * 2:(g + 1) * 2]
                    src = max_rows[gg].rearrange("(hl j c) p -> hl j (c p)", hl=4, j=2)
                sp.dma_start(dst.bitcast(F32), src).then_inc(maxt_loaded, 16)

            def spread_sums(gg, gpar):
                if first:
                    sp.wait_ge(sums_read, gg + 1)
                    src = sums_sb[0:P:32]
                else:
                    sp.wait_ge(ctx_read, gg + 1)
                    src = ctx_sb[DK:P:32, gpar]
                sp.dma_start(sum_rows[gg], src).then_inc(sums_stored, 16)
                sp.wait_ge(sums_stored, 16 * (gg + 1))
                sp.dma_start(sums_flat[:, :], sum_rows[gg].rearrange("j (p t) -> (j p) t", p=32)).then_inc(sums_loaded, 16)

            def store_inv(gg):
                sp.wait_ge(inv_done, gg + 1)
                sp.dma_start(inv_rows[gg].rearrange("j (p t) -> (j p) t", p=32), inv_flat[:, :]).then_inc(inv_stored, 16)

            def load_inv(gg):
                sp.wait_ge(inv_stored, 16 * (gg + 1))
                if due(gg):
                    sp.wait_ge(scaled, gg)
                sp.dma_start(inv_sum[:, :], inv_rows[gg].unsqueeze(1).broadcast_to([GROUP, 32, T])).then_inc(inv_loaded, 16)

            def load_resid(n):
                if first:
                    if due(n):
                        sp.wait_ge(proj_read["O"], 2 * n)
                    sp.dma_start(resid[:, :], x_in[n].rearrange("(c p) t -> p c t", p=P)).then_inc(resid_loaded, 16)
                else:
                    if due(n):
                        sp.wait_ge(out_stored, 16 * OUT_STORES * n)
                    else:
                        sp.wait_ge(y_set, 1)
                    src = x_in[n].rearrange("(g j r) t -> j r g t", j=GROUP, r=DK)
                    for j in range(GROUP):
                        sp.dma_start(y_tile[32 * j:32 * j + DK], src[j]).then_inc(resid_loaded, 16)

            def store_out(n):
                if first:
                    sp.wait_ge(proj_read["O"], 2 * (n + 1))
                    sp.dma_start(x_out[n].rearrange("(c p) t -> p c t", p=P), x1[:, :]).then_inc(out_stored, 16)
                else:
                    sp.wait_ge(added, G * (n + 1))
                    dst = x_out[n].rearrange("(g j r) t -> j r g t", j=GROUP, r=DK)
                    for j in range(GROUP):
                        sp.dma_start(dst[j], y_tile[32 * j:32 * j + DK]).then_inc(out_stored, 16)

            sp.dma_start(keep[:, :], mask).then_inc(consts_loaded, 16)
            sp.dma_start(bias_col[:, 0:1], bias.unsqueeze(0).broadcast_to([B, 1])).then_inc(consts_loaded, 16)
            sp.dma_start(ident[:, :], ident_in).then_inc(consts_loaded, 16)
            if first:
                sp.dma_start(w_o[:, :], w_out.rearrange("(c p) o -> p c o", p=P)).then_inc(consts_loaded, 16)
            else:
                sp.dma_start(unit[96:128, :], unit_rows).then_inc(consts_loaded, 16)
            sp.dma_start(keep_rows, mask).then_inc(consts_loaded, 16)
            load_x(0, 0)
            load_mask(0)
            for k in w_in:
                sp.dma_start(w_raw[k], w_in[k].rearrange("(c p) o -> p c o", p=P)).then_inc(w_loaded[k], 16)
            sp.wait_ge(x_split, 1)
            load_x(1, 1)
            sp.wait_ge(mrow_step, 4)
            sp.dma_start(mask_rows[0], mrow_hi[:, :]).then_inc(mrow_stored, 16)
            sp.dma_start(mask_rows[1], mrow_lo[:, :]).then_inc(mrow_stored, 16)
            for k in KINDS:
                store_parts(k, 0)
            sp.wait_ge(mrow_stored, 32)
            sp.wait_ge(consts_loaded, 16 * 5)
            if first:
                sp.wait_ge(tiles_set, 2)
            else:
                sp.wait_ge(q_set, 1)
                sp.wait_ge(k_set, 2)
            load_stack(0, 0, 0)
            sp.wait_ge(lo_done[MASKED], 2)
            load_mask(1)
            load_stack(0, 0, 1)
            for k in KINDS:
                store_parts(k, 1)
            if first:
                load_stack(1, 1, 0)
            else:
                sp.wait_ge(k_set, 3)
                sp.wait_ge(k_odd_set, 1)
            store_max(0, 0, 0)
            load_max(0, 0, 0)

            def parts_due(n, g):
                for k in KINDS:
                    if exists(n, 2) and max(s for s in UNITS if UNITS[s][0] == k) // KC + 1 == g:
                        store_parts(k, n + 2)

            def batch(n, par):
                if exists(n, 2):
                    sp.wait_ge(x_split, n + 2)
                    load_x(n + 2, par)
                if first and exists(n, 2):
                    sp.wait_ge(lo_done[MASKED], 2 * (n + 2))
                    load_mask(n + 2)
                for g in range(G):
                    before = n * G + g - 1
                    if due(before + 1):
                        spread_sums(before, (g - 1) % 2)
                    if first and g == 0:
                        if due(n - 1):
                            store_out(n - 2)
                        if due(n):
                            load_resid(n - 1)
                    if first and g == 1:
                        parts_due(n, g)
                        if exists(n, 2):
                            load_stack(n + 2, par, 0)
                    ready = [u[:3] for u in max_units(n, par, g) if completes(u)]
                    for u in ready:
                        store_max(*u)
                    if due(before + 1):
                        store_inv(before)
                    for u in ready:
                        load_max(*u)
                    if due(before + 1):
                        load_inv(before)
                    if first and g == 0 and exists(n, 1):
                        load_stack(n + 1, 1 - par, 1)
                    if not first:
                        if g == 0 and exists(n, 2):
                            sp.wait_ge(lo_done[MASKED], 2 * (n + 2))
                            load_mask(n + 2)
                        if g == 1:
                            if due(n):
                                store_out(n - 1)
                            load_resid(n)
                        parts_due(n, g)
                        if g in (0, 2) and exists(n, 1):
                            load_stack(n + 1, 1 - par, g // 2)

            batches(sp, batch)
            spread_sums(B * G - 1, (G - 1) % 2)
            store_inv(B * G - 1)
            load_inv(B * G - 1)
            if first:
                store_out(B - 2)
                load_resid(B - 1)
            store_out(B - 1)
            sp.wait_ge(out_stored, 16 * OUT_STORES * B)

        @block.gpsimd
        def _(pool):
            if first:
                pool.memset(ones[:, :], 1.0).then_inc(one_set, 1)
                pool.wait_ge(one_set, 1)
                pool.memset(q_tile[96:128].bitcast(F32), 1.0).then_inc(tiles_set, 1)
                pool.memset(k_tile[96:128].bitcast(F32), 1.0).then_inc(tiles_set, 1)
                pool.wait_ge(tiles_set, 2)
            else:
                pool.memset(v_tile[:, :], 1.0).then_inc(v_set, 1)
                pool.memset(y_tile[:, :], 0.0).then_inc(y_set, 1)
                pool.wait_ge(v_set, 1)
                pool.wait_ge(y_set, 1)
                pool.memset(q_tile[96:128].bitcast(F32), 1.0).then_inc(q_set, 1)
                pool.wait_ge(q_set, 1)

            def take_x_lo(n, par):
                pool.wait_ge(x_hi_done, n + 1)
                pool.tensor_tensor(x_lo[:, par], x_tile[:, :], x_hi[:, par].bitcast(F32), ALU.subtract).then_inc(x_split, 1)

            def split_unit(k, half, n):
                if k == MASKED:
                    pool.wait_ge(mask_loaded, 16 * (n + 1))
                    pool.wait_ge(proj_read[k], 2 * n + half + 1)
                    pool.tensor_tensor(raw[k][:, half], raw[k][:, half], mask_b[:, :], ALU.mult).then_inc(masked, 1)
                    pool.wait_ge(masked, 2 * n + half + 1)
                pool.wait_ge(hi_done[k], 2 * n + half + 1)
                if due(n):
                    pool.wait_ge(parts_stored[k], 32 * n)
                pool.tensor_tensor(lo[k][:, half], raw[k][:, half], hi[k][:, half].bitcast(F32), ALU.subtract).then_inc(lo_done[k], 1)

            def scale_context(n, par, g):
                gg = n * G + g
                pool.wait_ge(ctx_read, gg + 1)
                if first:
                    if due(n - 1):
                        pool.wait_ge(proj_full["O"], 2 * (n - 1))
                    pool.wait_ge(inv_loaded, 16 * (gg + 1))
                    pool.tensor_tensor(context[:, par, g], ctx_sb[:, g % 2], inv_sum[:, :], ALU.mult).then_inc(scaled, 1)
                else:
                    pool.wait_ge(inv_loaded, 16 * (gg + 1))
                    pool.tensor_tensor(ctx_sb[:, g % 2], ctx_sb[:, g % 2], inv_sum[:, :], ALU.mult).then_inc(scaled, 1)
                    pool.wait_ge(resid_loaded, 16 * RESID_LOADS * (n + 1))
                    pool.wait_ge(scaled, gg + 1)
                    pool.tensor_tensor(y_tile[:, g], ctx_sb[:, g % 2], y_tile[:, g], ALU.add).then_inc(added, 1)

            take_x_lo(0, 0)
            if not first:
                pool.wait_ge(x_split, 1)
                pool.memset(k_tile[0:96, 1].bitcast(F32), 0.0).then_inc(k_odd_set, 1)
                pool.wait_ge(k_odd_set, 1)
            take_x_lo(1, 1)
            for k in KINDS:
                for half in range(2):
                    split_unit(k, half, 0)
            for k in KINDS:
                for half in range(2):
                    split_unit(k, half, 1)

            def batch(n, par):
                for g in range(G):
                    for c in range(KC):
                        if g == 0 and c == SPLIT_STEP and exists(n, 2):
                            take_x_lo(n + 2, par)
                        unit_here = unit_of_step(n, g * KC + c)
                        if unit_here and unit_here[0] in KINDS:
                            split_unit(*unit_here)
                    if g > 0:
                        scale_context(n, par, g - 1)
                    elif due(n):
                        scale_context(n - 1, 1 - par, G - 1)

            batches(pool, batch)
            scale_context(B - 1, 1, G - 1)

        @block.scalar
        def _(act):
            def read_unit(kind, half, n, at=0):
                act.wait_ge(proj_full[kind], 2 * n + half + 1)
                if due(n):
                    act.wait_ge(lo_done[kind], 2 * n)
                act.activation(raw[kind][:, half], unit_bank[at][:, :], ACT.Copy).then_inc(proj_read[kind], 1)

            def read_v(half, n, par, at=0):
                act.wait_ge(proj_full["V"], 2 * n + half + 1)
                if due(n - 1):
                    act.wait_ge(pv_done, STEPS * (n - 1))
                act.activation(v_tile[:, par, 2 * half:2 * half + 2, :, 0:DK],
                               unit_bank[at][:, :].rearrange("p (c h d) -> p c h d", c=2, h=H), ACT.Copy).then_inc(proj_read["V"], 1)

            def take_hi(kind, half, n):
                if kind == MASKED:
                    act.wait_ge(masked, 2 * n + half + 1)
                else:
                    act.wait_ge(proj_read[kind], 2 * n + half + 1)
                if due(n):
                    act.wait_ge(parts_stored[kind], 32 * n)
                act.activation(hi[kind][:, half], raw[kind][:, half], ACT.Copy).then_inc(hi_done[kind], 1)

            def read_max(m, g):
                gg = m * G + g
                act.wait_ge(maxt_full, gg + 1)
                if due(gg):
                    act.wait_ge(maxt_stored, 16 * gg)
                act.activation(max_t[:, :], maxt_bank[0:2 * GROUP * QC, 0:P], ACT.Copy).then_inc(maxt_read, 1)

            def read_context(gg, gpar):
                act.wait_ge(pv_done, KC * (gg + 1))
                if first:
                    if due(gg):
                        act.wait_ge(sums_stored, 16 * gg)
                    act.activation(sums_sb[:, :], ctx_bank[1][:, :], ACT.Copy).then_inc(sums_read, 1)
                if due(gg - 1):
                    act.wait_ge(scaled if first else added, gg - 1)
                act.activation(ctx_sb[:, gpar], ctx_bank[0 if first else gpar][:, :], ACT.Copy).then_inc(ctx_read, 1)

            if not first:
                act.wait_ge(v_set, 1)
            for i, (kind, half, n) in enumerate(PROLOGUE):
                if kind == "V":
                    read_v(half, n, 0, i % 2)
                else:
                    read_unit(kind, half, n, i % 2)
                    take_hi(kind, half, n)
            read_max(0, 0)

            def batch(n, par):
                late = None
                for g in range(G):
                    done = [u for u in max_units(n, par, g) if completes(u)]
                    for c in range(KC):
                        step = n * STEPS + g * KC + c
                        for j in range(GROUP):
                            act.wait_ge(st_full, GROUP * step + j + 1)
                            if j == 0 and due(step - 1):
                                act.wait_ge(pv_done, step - 1)
                            act.activation(probs[:, (g * KC + c) % 2, j], st_bank[j % 2][:, :], ACT.Exp, scale=SCALE).then_inc(exp_done, 1)
                        if late:
                            take_hi(*late)
                            late = None
                        if c == 0 and due(n * G + g):
                            read_context(n * G + g - 1, (g - 1) % 2)
                        unit_here = unit_of_step(n, g * KC + c)
                        if unit_here and unit_here[0] == "V":
                            read_v(unit_here[1], unit_here[2], 1 - par)
                        elif unit_here and unit_here[0] in KINDS:
                            read_unit(*unit_here)
                            late = unit_here
                        if c == QC - AHEAD and done:
                            read_max(done[0][0], done[0][2])
                if late:
                    take_hi(*late)

            batches(act, batch)
            read_context(B * G - 1, (G - 1) % 2)

        @block.vector
        def _(dve):
            for n, k in enumerate(w_in):
                dve.wait_ge(w_loaded[k], 16)
                dve.tensor_copy(w_hi[k][:, :], w_raw[k]).then_inc(w_half, 1)
                dve.wait_ge(w_half, n + 1)
                dve.tensor_tensor(w_lo[k][:, :], w_raw[k], w_hi[k][:, :].bitcast(F32), ALU.subtract).then_inc(w_split, 1)
            def take_x_hi(n, par):
                dve.wait_ge(x_loaded, 16 * (n + 1))
                if due(n - 1):
                    dve.wait_ge(proj_full["V"], 2 * (n - 1))
                dve.tensor_copy(x_hi[:, par], x_tile[:, :]).then_inc(x_hi_done, 1)

            take_x_hi(0, 0)
            take_x_hi(1, 1)
            dve.wait_ge(consts_loaded, 16 * 5)
            dve.tensor_scalar(bias_col[:, 1:2], bias_col[:, 0:1], 0.0 if first else RSCALE, None, ALU.mult).then_inc(mrow_step, 1)
            dve.tensor_scalar(mrow[:, :], keep[:, :], -NEG * RSCALE, NEG * RSCALE, ALU.mult, ALU.add).then_inc(mrow_step, 1)
            dve.wait_ge(mrow_step, 2)
            if not first:
                dve.scalar_tensor_tensor(out=mrow[:, :], in0=keep[:, :], scalar=bias_col[:, 1:2], in1=mrow[:, :],
                                         op0=ALU.mult, op1=ALU.add).then_inc(bias_added, 1)
                dve.wait_ge(bias_added, 1)
            dve.tensor_copy(mrow_hi[:, :].bitcast(F32R), mrow[:, :]).then_inc(mrow_step, 1)
            dve.wait_ge(mrow_step, 3)
            dve.tensor_tensor(mrow_lo[:, :].bitcast(F32R), mrow[:, :], mrow_hi[:, :], ALU.subtract).then_inc(mrow_step, 1)
            if not first:
                for par in range(2):
                    if par == 0:
                        dve.memset(k_tile[0:96, par].bitcast(F32), 0.0).then_inc(k_set, 1)
                    view = k_tile[96:128, par].rearrange("p (s two) t -> p s two t", two=2)
                    for odd in range(2):
                        last = dve.tensor_copy(view[:, :, odd], unit[96:128, odd:odd + 1].unsqueeze(2).broadcast_to([32, H // 2, T]))
                    last.then_inc(k_set, 1)

            def maximum(m, g, qc, j):
                n = ((m * G + g) * QC + qc) * GROUP + j
                if qc == 0 and j == 0 and due(m * G + g - 1):
                    dve.wait_ge(max_split_done, m * G + g - 1)
                dve.wait_ge(s_full, n + 1)
                col = j * QC + qc if first else (j % 2) * 2 * QC + (j // 2) * QC + qc
                dve.tensor_reduce(row_max[:, g % 2, col:col + 1], s_bank[j % 2][:, :], AX.X, ALU.max).then_inc(max_done, 1)

            def split_max(m, g):
                gg = m * G + g
                dve.wait_ge(max_done, GROUP * QC * (gg + 1))
                if due(gg):
                    dve.wait_ge(maxt_full, gg)
                outer = 1 if first else 2
                view = max_split[:, :].rearrange("p (o hl r) -> p hl o r", o=outer, hl=2)
                src = row_max[:, g % 2].rearrange("p (o r) -> p o r", o=outer)
                dve.tensor_scalar(view[:, 0].bitcast(F32R), src, -1.0, None, ALU.mult).then_inc(max_neg, 1)
                dve.wait_ge(max_neg, gg + 1)
                dve.scalar_tensor_tensor(out=view[:, 1].bitcast(F32R), in0=src, scalar=-1.0, in1=view[:, 0],
                                         op0=ALU.mult, op1=ALU.subtract).then_inc(max_split_done, 1)

            def invert_sums(gg):
                dve.wait_ge(sums_loaded, 16 * (gg + 1))
                if due(gg):
                    dve.wait_ge(inv_stored, 16 * gg)
                dve.reciprocal(inv_flat[:, :], sums_flat[:, :]).then_inc(inv_done, 1)

            def add_resid(half, n):
                dve.wait_ge(resid_loaded, 16 * (n + 1))
                dve.wait_ge(proj_full["O"], 2 * n + half + 1)
                if due(n):
                    dve.wait_ge(out_stored, 16 * n)
                dve.tensor_tensor(x1[:, half], proj_bank[:, :], resid[:, half], ALU.add).then_inc(proj_read["O"], 1)

            for m, mp, g, qc, j in first_units():
                maximum(m, g, qc, j)
                if completes((m, mp, g, qc, j)):
                    split_max(m, g)

            def batch(n, par):
                for g in range(G):
                    for c in range(KC):
                        for u in units_of_step(n, par, g, c):
                            maximum(u[0], *u[2:])
                            if completes(u):
                                split_max(u[0], u[2])
                        if g == 0 and c == SPLIT_STEP and exists(n, 2):
                            take_x_hi(n + 2, par)
                        if c == INV_STEP and due(n * G + g):
                            invert_sums(n * G + g - 1)
                        unit_here = unit_of_step(n, g * KC + c)
                        if unit_here and unit_here[0] == "O":
                            add_resid(*unit_here[1:])

            batches(dve, batch)
            invert_sums(B * G - 1)
            if first:
                for half in range(2):
                    add_resid(half, B - 1)

        @block.tensor
        def _(pe):
            tenant = [None, None]

            def project(kind, half, n, par, at=0):
                if tenant[at]:
                    pe.wait_ge(*tenant[at])
                tenant[at] = (proj_read[kind], 2 * n + half + 1)
                bank = unit_bank[at]
                if kind == "O":
                    pe.wait_ge(scaled, G * (n + 1))
                    jobs = [(bank[:, :], w_o[:, c, half * P:(half + 1) * P], context[:, par, c], c == 0, c == C - 1) for c in range(C)]
                else:
                    pe.wait_ge(x_split, n + 1)
                    w = SOURCE[kind]
                    pairs = [(c, x, wp) for c in range(C) for x, wp in ((x_hi, w_hi[w]), (x_lo, w_hi[w]), (x_hi, w_lo[w]))]
                    if kind == "V":
                        jobs = [(bank[:, t * D:(t + 1) * D], x[:, par, c, (2 * half + t) * P:(2 * half + t + 1) * P], wp[:, c], i == 0, i == 3 * C - 1)
                                for t in range(2) for i, (c, x, wp) in enumerate(pairs)]
                    else:
                        jobs = [(bank[:, :], wp[:, c, half * P:(half + 1) * P], x[:, par, c], i == 0, i == 3 * C - 1)
                                for i, (c, x, wp) in enumerate(pairs)]
                for i, (out, lhs_t, rhs, start, stop) in enumerate(jobs):
                    done = pe.matmul(out, lhs_t, rhs, start=start, stop=stop)
                    if i == len(jobs) - 1:
                        done.then_inc(proj_full[kind], 1)
                    if (i + 1) * GROUP // len(jobs) > i * GROUP // len(jobs):
                        yield

            def scores(m, mp, g, qc, j):
                n = ((m * G + g) * QC + qc) * GROUP + j
                h = g * GROUP + j
                if g % (G // STACKS) == 0 and qc == 0 and j == 0:
                    pe.wait_ge(stack_loaded[g * STACKS // G, ("even", "odd")[mp]], 8 * RAW_LOADS * (m - mp + 2))
                if due(n - 1):
                    pe.wait_ge(max_done, n - 1)
                pe.matmul(s_bank[j % 2][:, :], q_tile[0:MAX_ROW, mp, q_slot(h), qc * P:(qc + 1) * P],
                          k_tile[0:MAX_ROW, mp, h], start=True, stop=True).then_inc(s_full, 1)

            def transpose_max(m, g):
                gg = m * G + g
                pe.wait_ge(max_split_done, gg + 1)
                if due(gg):
                    pe.wait_ge(maxt_read, gg)
                pe.matmul(maxt_bank[0:2 * GROUP * QC, 0:P], max_split[:, :], ident[:, :], start=True, stop=True).then_inc(maxt_full, 1)

            def scores_t(n, par, g, c, j):
                unit_no = GROUP * (n * STEPS + g * KC + c) + j
                h = g * GROUP + j
                if c == 0 and j == 0:
                    pe.wait_ge(maxt_loaded, 16 * (n * G + g + 1))
                if due(unit_no - 1):
                    pe.wait_ge(exp_done, unit_no - 1)
                pe.matmul(st_bank[j % 2][:, :], k_tile[0:ROWS, par, h, c * P:(c + 1) * P],
                          q_tile[0:ROWS, par, q_slot(h)], start=True, stop=True).then_inc(st_full, 1)

            def attend(n, par, g, c):
                step = n * STEPS + g * KC + c
                gg = n * G + g
                pe.wait_ge(exp_done, GROUP * (step + 1))
                if c == 0:
                    pe.wait_ge(proj_read["V"], 2 * (n + 1))
                    if due(gg if first else gg - 1):
                        pe.wait_ge(ctx_read, gg if first else gg - 1)
                    if first and due(gg):
                        pe.wait_ge(sums_read, gg)
                bank = ctx_bank[0 if first else g % 2]
                for j in range(GROUP):
                    last = pe.matmul(bank[32 * j:32 * j + 32, :], v_tile[:, par, c, g * GROUP + j],
                                     probs[:, (g * KC + c) % 2, j], start=c == 0, stop=c == KC - 1)
                if first:
                    for j in range(GROUP):
                        last = pe.matmul(ctx_bank[1][32 * j:32 * j + 32, :], ones[:, :],
                                         probs[:, (g * KC + c) % 2, j], start=c == 0, stop=c == KC - 1)
                last.then_inc(pv_done, 1)

            pe.wait_ge(w_split, len(w_in))
            for i, (kind, half, n) in enumerate(PROLOGUE):
                for _ in project(kind, half, n, n % 2, i % 2):
                    pass
            if first:
                pe.wait_ge(tiles_set, 2)
            else:
                pe.wait_ge(q_set, 1)
                pe.wait_ge(k_set, 3)
                pe.wait_ge(k_odd_set, 1)
            pe.wait_ge(consts_loaded, 16 * 5)
            for u in first_units():
                scores(*u)
            transpose_max(0, 0)
            pe.wait_ge(*tenant[1])

            def batch(n, par):
                if not isinstance(n, int) or n == B - 2:
                    if par == 0:
                        tenant[0] = (proj_read["O"], 2 * n - 2) if first else (proj_read["K"], 2 * (n + 1) + 2)
                for g in range(G):
                    pending = None
                    for c in range(KC):
                        units = units_of_step(n, par, g, c)
                        unit_here = unit_of_step(n, g * KC + c)
                        pieces = iter(())
                        if unit_here:
                            kind, half, m = unit_here
                            pieces = project(kind, half, m, 1 - par if kind in "VO" else par)
                        for j in range(GROUP):
                            for u in units[len(units) * j // GROUP:len(units) * (j + 1) // GROUP]:
                                scores(*u)
                                if completes(u):
                                    pending = (u[0], u[2])
                            scores_t(n, par, g, c, j)
                            if j == 1:
                                if c > 0:
                                    attend(n, par, g, c - 1)
                                elif g > 0:
                                    attend(n, par, g - 1, KC - 1)
                                elif due(n):
                                    attend(n - 1, 1 - par, G - 1, KC - 1)
                            if j > 0:
                                next(pieces, None)
                        for _ in pieces:
                            pass
                        if c == QC - AHEAD and pending:
                            transpose_max(*pending)
                            pending = None

            batches(pe, batch)
            attend(B - 1, 1, G - 1, KC - 1)
            if first:
                for half in range(2):
                    for _ in project("O", half, B - 1, 1):
                        pass


def build(nc, x, mask, wq0_t, wo0_t, wq1_t, wk1_t, wv1_t, bias, unit_rows, ident, out):
    x1 = nc.dram_tensor("x1_scratch", x.shape, F32, kind="Internal").ap()
    build_layer(nc, 0, x, mask, bias, {"Q": wq0_t}, wo0_t, None, ident, x1)
    build_layer(nc, 1, x1, mask, bias, {"Q": wq1_t, "K": wk1_t, "V": wv1_t}, None, unit_rows, ident, out)


def kernel(x, cond_2048, L0_cond_Wq, L0_cond_Wo, L1_cond_Wq, L1_cond_Wk, L1_cond_Wv, L1_cond_b):
    import concourse.bacc as bacc
    import numpy as np
    from concourse.bass_utils import run_bass_kernel_spmd

    unit_rows = np.zeros((32, 2), np.float32)
    unit_rows[2:4, 0] = 1.0
    unit_rows[4:6, 1] = 1.0
    arrays = {
        "x": np.ascontiguousarray(x),
        "mask": np.ascontiguousarray(cond_2048),
        "wq0_t": np.ascontiguousarray(np.transpose(L0_cond_Wq)),
        "wo0_t": np.ascontiguousarray(np.transpose(L0_cond_Wo)),
        "wq1_t": np.ascontiguousarray(np.transpose(L1_cond_Wq)),
        "wk1_t": np.ascontiguousarray(np.transpose(L1_cond_Wk)),
        "wv1_t": np.ascontiguousarray(np.transpose(L1_cond_Wv)),
        "bias": np.ascontiguousarray(L1_cond_b),
        "unit_rows": unit_rows,
        "ident": np.eye(P, dtype=np.float32),
    }
    nc = bacc.Bacc("TRN2", target_bir_lowering=False, num_devices=1)
    args = [nc.dram_tensor(f"in_{k}", a.shape, F32, kind="ExternalInput").ap() for k, a in arrays.items()]
    args.append(nc.dram_tensor("out", arrays["x"].shape, F32, kind="ExternalOutput").ap())
    build(nc, *args)
    result = run_bass_kernel_spmd(nc, [{f"in_{k}": a for k, a in arrays.items()}], core_ids=[0])
    return result.results[0]["out"]
```
